# Optimizing a Trainium2 kernel written in Bass

```python
import numpy as np
import jax
import jax.numpy as jnp

def _softmax(x, axis=-1):
    return jax.nn.softmax(x, axis=axis)

def _gelu(x):
    return jax.nn.gelu(x, approximate=True)

def _silu(x):
    return jax.nn.silu(x)

def _sigmoid(x):
    return jax.nn.sigmoid(x)

def _layernorm(x, axis=-1, eps=1e-05):
    m = jnp.mean(x, axis=axis, keepdims=True)
    v = jnp.var(x, axis=axis, keepdims=True)
    return (x - m) / jnp.sqrt(v + eps)

def _scatter_add(tgt, idx, src, axis=0):
    return tgt.at[idx].add(src)

def _segment_sum(src, seg, n):
    return jax.ops.segment_sum(src, seg, n)
kernel_name = 'mk_dlrm_tower_d1_rec_r8_f8644c'

def setup_inputs(seed: int=0):
    np.random.seed(seed)
    _w = jnp.asarray

    def _rec_inputs():
        import jax
        import jax.numpy as jnp
        _tk = jax.random.key(seed)
        ids = jnp.stack([jax.random.randint(jax.random.fold_in(_tk, 200 + f), (2048,), 0, v, jnp.int32) for f, v in enumerate([1000, 12500, 12500, 12500, 12500, 1000, 1250, 125000, 1250, 1000, 1000, 1000, 12500, 1000, 1250, 1250, 1250, 1000, 1000, 1000, 12500, 1250, 1000, 12500, 1250, 1000])], axis=1)
        tbl_0 = 0.05 * jax.random.normal(jax.random.fold_in(_tk, 500 + 0), (1000, 128), jnp.float32)
        tbl_1 = 0.05 * jax.random.normal(jax.random.fold_in(_tk, 500 + 1), (12500, 128), jnp.float32)
        tbl_2 = 0.05 * jax.random.normal(jax.random.fold_in(_tk, 500 + 2), (12500, 128), jnp.float32)
        tbl_3 = 0.05 * jax.random.normal(jax.random.fold_in(_tk, 500 + 3), (12500, 128), jnp.float32)
        tbl_4 = 0.05 * jax.random.normal(jax.random.fold_in(_tk, 500 + 4), (12500, 128), jnp.float32)
        tbl_5 = 0.05 * jax.random.normal(jax.random.fold_in(_tk, 500 + 5), (1000, 128), jnp.float32)
        tbl_6 = 0.05 * jax.random.normal(jax.random.fold_in(_tk, 500 + 6), (1250, 128), jnp.float32)
        tbl_7 = 0.05 * jax.random.normal(jax.random.fold_in(_tk, 500 + 7), (125000, 128), jnp.float32)
        tbl_8 = 0.05 * jax.random.normal(jax.random.fold_in(_tk, 500 + 8), (1250, 128), jnp.float32)
        tbl_9 = 0.05 * jax.random.normal(jax.random.fold_in(_tk, 500 + 9), (1000, 128), jnp.float32)
        tbl_10 = 0.05 * jax.random.normal(jax.random.fold_in(_tk, 500 + 10), (1000, 128), jnp.float32)
        tbl_11 = 0.05 * jax.random.normal(jax.random.fold_in(_tk, 500 + 11), (1000, 128), jnp.float32)
        tbl_12 = 0.05 * jax.random.normal(jax.random.fold_in(_tk, 500 + 12), (12500, 128), jnp.float32)
        tbl_13 = 0.05 * jax.random.normal(jax.random.fold_in(_tk, 500 + 13), (1000, 128), jnp.float32)
        tbl_14 = 0.05 * jax.random.normal(jax.random.fold_in(_tk, 500 + 14), (1250, 128), jnp.float32)
        tbl_15 = 0.05 * jax.random.normal(jax.random.fold_in(_tk, 500 + 15), (1250, 128), jnp.float32)
        tbl_16 = 0.05 * jax.random.normal(jax.random.fold_in(_tk, 500 + 16), (1250, 128), jnp.float32)
        tbl_17 = 0.05 * jax.random.normal(jax.random.fold_in(_tk, 500 + 17), (1000, 128), jnp.float32)
        tbl_18 = 0.05 * jax.random.normal(jax.random.fold_in(_tk, 500 + 18), (1000, 128), jnp.float32)
        tbl_19 = 0.05 * jax.random.normal(jax.random.fold_in(_tk, 500 + 19), (1000, 128), jnp.float32)
        tbl_20 = 0.05 * jax.random.normal(jax.random.fold_in(_tk, 500 + 20), (12500, 128), jnp.float32)
        tbl_21 = 0.05 * jax.random.normal(jax.random.fold_in(_tk, 500 + 21), (1250, 128), jnp.float32)
        tbl_22 = 0.05 * jax.random.normal(jax.random.fold_in(_tk, 500 + 22), (1000, 128), jnp.float32)
        tbl_23 = 0.05 * jax.random.normal(jax.random.fold_in(_tk, 500 + 23), (12500, 128), jnp.float32)
        tbl_24 = 0.05 * jax.random.normal(jax.random.fold_in(_tk, 500 + 24), (1250, 128), jnp.float32)
        tbl_25 = 0.05 * jax.random.normal(jax.random.fold_in(_tk, 500 + 25), (1000, 128), jnp.float32)
        _rk = jax.random.fold_in(_tk, 7)
        r_dense_features = -0.000520686 + 1.00062 * jax.random.normal(jax.random.fold_in(_rk, 101), (2048, 128), jnp.float32)
        W_top1 = 0.0405887 * jax.random.normal(jax.random.fold_in(_tk, 801), (607, 512), jnp.float32)
        W_top2 = 0.0441942 * jax.random.normal(jax.random.fold_in(_tk, 802), (512, 256), jnp.float32)
        W_top3 = 0.0625 * jax.random.normal(jax.random.fold_in(_tk, 803), (256, 1), jnp.float32)
        b_top1 = jnp.zeros((512,), jnp.float32)
        b_top2 = jnp.zeros((256,), jnp.float32)
        return (r_dense_features, ids, tbl_0, tbl_1, tbl_2, tbl_3, tbl_4, tbl_5, tbl_6, tbl_7, tbl_8, tbl_9, tbl_10, tbl_11, tbl_12, tbl_13, tbl_14, tbl_15, tbl_16, tbl_17, tbl_18, tbl_19, tbl_20, tbl_21, tbl_22, tbl_23, tbl_24, tbl_25, W_top1, b_top1, W_top2, b_top2, W_top3)
    r_dense_features, ids, tbl_0, tbl_1, tbl_2, tbl_3, tbl_4, tbl_5, tbl_6, tbl_7, tbl_8, tbl_9, tbl_10, tbl_11, tbl_12, tbl_13, tbl_14, tbl_15, tbl_16, tbl_17, tbl_18, tbl_19, tbl_20, tbl_21, tbl_22, tbl_23, tbl_24, tbl_25, W_top1, b_top1, W_top2, b_top2, W_top3 = _rec_inputs()

    def _L0_rec_setup():
        import jax, jax.numpy as jnp
        import numpy as np
        F = 26
        N = F + 1
        _TRIU_I, _TRIU_J = np.triu_indices(N, k=1)
        key = jax.random.key(seed)
        k1, k2 = jax.random.split(key)
        B, D = (2048, 128)
        dense_features = jax.random.normal(k1, (B, D), dtype=jnp.float32)
        sparse_features = jax.random.normal(k2, (B, F, D), dtype=jnp.float32)
        return {'dense_features': dense_features, 'sparse_features': sparse_features}
    _L0_rec_all = _L0_rec_setup()
    _L0_rec_in = {k: v for k, v in _L0_rec_all.items() if k in ()}
    del _L0_rec_all
    return {'r_dense_features': r_dense_features, 'ids': ids, 'tbl_0': tbl_0, 'tbl_1': tbl_1, 'tbl_2': tbl_2, 'tbl_3': tbl_3, 'tbl_4': tbl_4, 'tbl_5': tbl_5, 'tbl_6': tbl_6, 'tbl_7': tbl_7, 'tbl_8': tbl_8, 'tbl_9': tbl_9, 'tbl_10': tbl_10, 'tbl_11': tbl_11, 'tbl_12': tbl_12, 'tbl_13': tbl_13, 'tbl_14': tbl_14, 'tbl_15': tbl_15, 'tbl_16': tbl_16, 'tbl_17': tbl_17, 'tbl_18': tbl_18, 'tbl_19': tbl_19, 'tbl_20': tbl_20, 'tbl_21': tbl_21, 'tbl_22': tbl_22, 'tbl_23': tbl_23, 'tbl_24': tbl_24, 'tbl_25': tbl_25, 'W_top1': W_top1, 'b_top1': b_top1, 'W_top2': W_top2, 'b_top2': b_top2, 'W_top3': W_top3}

def reference(r_dense_features, ids, tbl_0, tbl_1, tbl_2, tbl_3, tbl_4, tbl_5, tbl_6, tbl_7, tbl_8, tbl_9, tbl_10, tbl_11, tbl_12, tbl_13, tbl_14, tbl_15, tbl_16, tbl_17, tbl_18, tbl_19, tbl_20, tbl_21, tbl_22, tbl_23, tbl_24, tbl_25, W_top1, b_top1, W_top2, b_top2, W_top3):
    import jax
    import jax.numpy as jnp

    def _L0_rec_ref(dense_features, sparse_features):
        import jax, jax.numpy as jnp
        import numpy as np
        F = 26
        N = F + 1
        _TRIU_I, _TRIU_J = np.triu_indices(N, k=1)
        combined = jnp.concatenate([dense_features[:, None, :], sparse_features], axis=1)
        interactions = jnp.einsum('bnd,bmd->bnm', combined, combined)
        interactions_flat = interactions[:, _TRIU_I, _TRIU_J]
        return jnp.concatenate([dense_features, interactions_flat], axis=1)
    e = jnp.stack([tbl_0[ids[:, 0]], tbl_1[ids[:, 1]], tbl_2[ids[:, 2]], tbl_3[ids[:, 3]], tbl_4[ids[:, 4]], tbl_5[ids[:, 5]], tbl_6[ids[:, 6]], tbl_7[ids[:, 7]], tbl_8[ids[:, 8]], tbl_9[ids[:, 9]], tbl_10[ids[:, 10]], tbl_11[ids[:, 11]], tbl_12[ids[:, 12]], tbl_13[ids[:, 13]], tbl_14[ids[:, 14]], tbl_15[ids[:, 15]], tbl_16[ids[:, 16]], tbl_17[ids[:, 17]], tbl_18[ids[:, 18]], tbl_19[ids[:, 19]], tbl_20[ids[:, 20]], tbl_21[ids[:, 21]], tbl_22[ids[:, 22]], tbl_23[ids[:, 23]], tbl_24[ids[:, 24]], tbl_25[ids[:, 25]]], axis=1)
    z = _L0_rec_ref(r_dense_features, e)
    z = z.reshape(z.shape[0], -1)
    h = jnp.concatenate([z, r_dense_features], axis=1)
    h = jnp.maximum(h @ W_top1 + b_top1, 0.0)
    h = jnp.maximum(h @ W_top2 + b_top2, 0.0)
    y = h @ W_top3
    return y

_drawn_inputs = setup_inputs


def setup_inputs(seed=0):
    import zlib

    import numpy as np

    out = dict(_drawn_inputs(seed))
    spreads = {'b_top1': (0.0, 0.1), 'b_top2': (0.0, 0.1)}
    factors = {}
    for name, (base, spread) in spreads.items():
        noise = np.random.default_rng([zlib.crc32(name.encode()), seed]).standard_normal(out[name].shape)
        drawn = base * np.exp(spread * noise) if base else spread * noise
        out[name] = jnp.asarray(drawn.astype(out[name].dtype))
    for name, factor in factors.items():
        out[name] = (out[name] * factor).astype(out[name].dtype)
    return out
```

```python
from contextlib import ExitStack

import concourse.bass as bass
from concourse import mybir

F32 = mybir.dt.float32
F32R = mybir.dt.float32r
I32 = mybir.dt.int32
U32 = mybir.dt.uint32
ALU = mybir.AluOpType
ACT = mybir.ActivationFunctionType

P = 128
SUB = 128
UNIT = 2 * SUB
HOT = (0, 5, 9, 10, 11, 13, 17)
NTAB = 26
NF = NTAB + 1
COLD = tuple(t for t in range(NTAB) if t not in HOT)
ORDER = (0,) + tuple(1 + t for t in COLD) + tuple(1 + t for t in HOT)
NCOLD, NHOT = len(COLD), len(HOT)
NPAIR = NF * (NF - 1) // 2
ZCH = 3
ZP = NPAIR // ZCH
PB = 4
BATCHES = [list(range(k, min(k + PB, NCOLD + 1))) for k in range(0, NCOLD + 1, PB)]
NB = len(BATCHES)
SLOT = 32
QUADS = SUB // 4
GQ = 8
GB = QUADS // GQ
LOW = NF // 2


def pair_rows():
    at, k = {}, P
    for a in range(NF):
        for b in range(a + 1, NF):
            at[a, b] = k
            k += 1
    return [at[min(ORDER[n], ORDER[m]), max(ORDER[n], ORDER[m])] for n in range(NF) for m in range(n + 1, NF)]


def pair_runs():
    runs, at = [], 0
    for n in range(NF - 1):
        m, left = n, NF - 1 - n
        while left:
            k = min(left, ZP - at % ZP)
            runs.append((n, m, at // ZP, at % ZP, k))
            at, m, left = at + k, m + k, left - k
    return runs


RUNS = pair_runs()


def reached(eng, semaphore, value):
    if not isinstance(value, int) or value > 0:
        eng.wait_ge(semaphore, value)


def settle(eng, passed):
    eng.sem_inc(passed, 1)


def dlrm(nc, dense, ids, ids_by_table, tables, W1, b1, W2, b2, W3, out):
    B, D = dense.shape
    H1, H2 = W2.shape
    O1, O2 = H1 // P, H2 // P
    NU = B // UNIT
    GROUPS = O1 + O2 + 1
    CH = {t: -(-tables[t].shape[0] // P) for t in HOT}
    assert len(set(CH.values())) == 1
    NCH = CH[HOT[0]]
    TP = tables[HOT[0]].shape[0] // NCH
    assert TP * NCH == tables[HOT[0]].shape[0] and D == P
    HC = NCH // 2
    PIECES = 2 * NHOT

    scratch = nc.dram_tensor("gram_scratch", [2, NF - 1, NF - 1, UNIT], F32, kind="Internal").ap()

    with ExitStack() as ctx:
        def sb(name, shape, dt=F32):
            return ctx.enter_context(nc.sbuf_tensor(name, shape, dt))

        def ps(name, shape, dt=F32):
            return ctx.enter_context(nc.psum_tensor(name, shape, dt))

        def sem(name):
            return ctx.enter_context(nc.semaphore(name))

        ident = sb("ident", [P, P])
        row_number = sb("row_number", [P, NCH])
        w1 = sb("w1", [P, 1 + ZCH, H1])
        w1_tail = sb("w1_tail", [P, H1])
        w2 = sb("w2", [P, O1, H2])
        w3 = sb("w3", [P, O2])
        bias1 = sb("bias1", [P, O1])
        bias2 = sb("bias2", [P, O2])
        hot_hi = sb("hot_hi", [P, NHOT, NCH, D], F32R)
        hot_lo = sb("hot_lo", [P, NHOT, NCH, D], F32R)
        ids_sb = sb("ids_sb", [P, 2, 2, NTAB], I32)
        rows = sb("rows", [P, 2, 1 + NCOLD, D])
        hot_ids = sb("hot_ids", [P, NHOT, UNIT], I32)
        onehot = sb("onehot", [P, 2, HC, UNIT], F32R)
        feats = sb("feats", [P, 4, SUB, SLOT])
        gram = sb("gram", [P, NF - 1, SUB])
        z = sb("z", [P, 2, ZCH, UNIT])
        h1 = sb("h1", [P, O1, UNIT])
        h2 = sb("h2", [P, O2, UNIT])
        y = sb("y", [1, UNIT])

        turned = ps("turned", [P, 2, PB, P])
        sums = ps("sums", [P, 2, 2 * UNIT])
        quads = ps("quads", [P, 2, GQ, P])

        ident_zero, ident_ready, rownum_ready = sem("ident_zero"), sem("ident_ready"), sem("rownum_ready")
        pad_ready = sem("pad_ready")
        w_loaded = sem("w_loaded")
        w1_merged = sem("w1_merged")
        staged = [sem(f"staged{t}") for t in range(NHOT)]
        hi_ready, hot_ready = sem("hi_ready"), sem("hot_ready")
        sp_passed, pool_passed = sem("sp_passed"), sem("pool_passed")
        ids_loaded = [sem("ids_loaded0"), sem("ids_loaded1")]
        dense_loaded = [sem(f"dense_loaded{a}") for a in range(2)]
        rows_loaded = [[sem(f"rows_loaded{a}_{k}") for k in range(NB)] for a in range(2)]
        hot_ids_loaded = sem("hot_ids_loaded")
        turned_ready, turned_taken = sem("turned_ready"), sem("turned_taken")
        onehot_ready, onehot_used = sem("onehot_ready"), sem("onehot_used")
        sum_ready, sum_taken = sem("sum_ready"), sem("sum_taken")
        quads_ready, quads_taken_v, quads_taken_s = sem("quads_ready"), sem("quads_taken_v"), sem("quads_taken_s")
        gram_stored = sem("gram_stored")
        z_loaded = [sem("z_loaded0"), sem("z_loaded1")]
        y_free = sem("y_free")

        def stage(t):
            per_buffer = SUB * SLOT // (NCH * D)
            at = t % per_buffer * NCH * D
            return feats[0:TP, 2 + t // per_buffer, :, :].rearrange("p s f -> p (s f)")[:, at:at + NCH * D]

        def sums_before(u):
            return 2 * NHOT + (NHOT + GROUPS) * (u - 1)

        def features(q, first, count):
            return feats[:, q, :, first:first + count].rearrange("p s f -> p f s")

        block = ctx.enter_context(nc.Block())

        @block.sync
        def _(sp):
            def load_ids(u, par):
                reached(sp, onehot_ready, PIECES * u)
                settle(sp, sp_passed)
                sp.dma_start(hot_ids[0:TP, :, :],
                             ids_by_table[0:NHOT, bass.ds(u * UNIT, UNIT)].unsqueeze(0).to_broadcast([TP, NHOT, UNIT])
                             ).then_inc(hot_ids_loaded, 16)
                for k in range(NB):
                    for a in range(2):
                        reached(sp, rows_loaded[a][k], 16 * sum(f > 0 for f in BATCHES[k]) * (u - 1))
                    settle(sp, sp_passed)
                sp.dma_start(ids_sb[:, par, :, :],
                             ids[bass.ds(u * UNIT, UNIT), :].rearrange("(a p) f -> p a f", p=P)
                             ).then_inc(ids_loaded[par], 16)

            def load_dense(u, a):
                reached(sp, turned_ready, 2 * NB * u - 2 * NB + a * NB + 1)
                settle(sp, sp_passed)
                sp.dma_start(rows[:, a, 0, :], dense[bass.ds(u * UNIT + a * SUB, SUB), :]
                             ).then_inc(dense_loaded[a], 16)

            def load_pairs(u, par):
                sp.wait_ge(gram_stored, 64 * u + 64)
                settle(sp, sp_passed)
                for n, m, c, p, k in RUNS:
                    sp.dma_start(z[p:p + k, par, c, :], scratch[par, n, m:m + k, :]).then_inc(z_loaded[par], 16)

            def step(u, par, first, more):
                if more:
                    load_ids(u + 1, 1 - par)
                if not first:
                    load_pairs(u - 1, 1 - par)
                if not isinstance(u, int) or u > 0:
                    sp.wait_ge(sum_ready, sums_before(u))
                    settle(sp, sp_passed)
                for a in range(2):
                    if more:
                        load_dense(u + 1, a)
                    reached(sp, quads_taken_v, 2 * GB * u + (a + 1) * GB)
                    reached(sp, quads_taken_s, 2 * GB * u + (a + 1) * GB)
                    settle(sp, sp_passed)
                    for n0, n1 in ((0, LOW), (LOW, NF - 1)):
                        sp.dma_start(scratch[par, n0:n1, n0:, a * SUB:(a + 1) * SUB], gram[n0:n1, n0:, :]
                                     ).then_inc(gram_stored, 16)

            load_ids(0, 0)
            load_dense(0, 0)
            load_dense(0, 1)
            for t in range(NHOT):
                sp.dma_start(stage(t), tables[HOT[t]].rearrange("(p c) d -> p (c d)", c=NCH)).then_inc(staged[t], 16)
            sp.dma_start(w1[:, 0, :], W1[0:P, :]).then_inc(w_loaded, 16)
            sp.dma_start(w1_tail[:, :], W1[P + NPAIR:2 * P + NPAIR, :]).then_inc(w_loaded, 16)
            sp.dma_start(w1[0:ZP, 1:1 + ZCH, :], W1[P:P + NPAIR, :].rearrange("(c p) n -> p c n", p=ZP)
                         ).then_inc(w_loaded, 16)
            sp.dma_start(w2[:, :, :], W2.rearrange("(c p) n -> p c n", p=P)).then_inc(w_loaded, 16)
            sp.dma_start(w3[:, :], W3).then_inc(w_loaded, 16)
            sp.dma_start(bias1[:, :], b1).then_inc(w_loaded, 16)
            sp.dma_start(bias2[:, :], b2).then_inc(w_loaded, 16)
            step(0, 0, True, True)
            with sp.Fori(0, (NU - 2) // 2) as i:
                step(2 * i + 1, 1, False, True)
                step(2 * i + 2, 0, False, True)
            step(NU - 1, 1, False, False)
            load_pairs(NU - 1, 1)

        @block.gpsimd
        def _(pool):
            nc.gpsimd.memset(ident[:, :], 0.0).then_inc(ident_zero, 1)
            pool.wait_ge(ident_zero, 1)
            nc.gpsimd.affine_select(out=ident[:, :], in_=ident[:, :], compare_op=ALU.not_equal, fill=1.0, base=0,
                                    pattern=[[-1, P]], channel_multiplier=1).then_inc(ident_ready, 1)
            nc.gpsimd.iota(row_number[:, :], pattern=[[1, NCH]], base=0, channel_multiplier=NCH,
                           allow_small_or_imprecise_dtypes=True).then_inc(rownum_ready, 1)

            def step(u, par, j):
                reached(pool, ids_loaded[par], 16 * j + 16)
                settle(pool, pool_passed)
                for a in range(2):
                    for k, batch in enumerate(BATCHES):
                        reached(pool, turned_ready, 2 * NB * u - 2 * NB + a * NB + k + 1)
                        settle(pool, pool_passed)
                        for f in batch:
                            if f == 0:
                                continue
                            t = COLD[f - 1]
                            nc.gpsimd.indirect_dma_start(
                                out=rows[:, a, f, :], out_offset=None, in_=tables[t],
                                in_offset=bass.IndirectOffsetOnAxis(ap=ids_sb[:, par, a, t:t + 1].bitcast(U32), axis=0),
                            ).then_inc(rows_loaded[a][k], 16)

            step(0, 0, 0)
            with pool.Fori(0, (NU - 2) // 2) as i:
                step(2 * i + 1, 1, i)
                step(2 * i + 2, 0, i + 1)
            step(NU - 1, 1, NU // 2 - 1)

        @block.tensor
        def _(pe):
            def transposes(u, par, a):
                for k, batch in enumerate(BATCHES):
                    if k == 0:
                        pe.wait_ge(dense_loaded[a], 16 * u + 16)
                    pe.wait_ge(rows_loaded[a][k], 16 * sum(f > 0 for f in batch) * (u + 1))
                    reached(pe, turned_taken, 2 * NB * u + a * NB + k - 1)
                    for n, f in enumerate(batch):
                        last = nc.tensor.transpose(turned[:, (a * NB + k) % 2, n, :], rows[:, a, f, :], ident[:, :])
                    last.then_inc(turned_ready, 1)

            def lookups(u, n, bank):
                for t in range(NHOT):
                    reached(pe, sum_taken, n + t - 1)
                    for c2 in range(2):
                        pe.wait_ge(onehot_ready, PIECES * u + 2 * t + c2 + 1)
                        for c in range(HC):
                            chunk = c2 * HC + c
                            nc.tensor.matmul(sums[:, (bank + t) % 2, 0:UNIT], hot_hi[0:TP, t, chunk, :],
                                             onehot[0:TP, c2, c, :], start=(chunk == 0), stop=False)
                            last = nc.tensor.matmul(sums[:, (bank + t) % 2, 0:UNIT], hot_lo[0:TP, t, chunk, :],
                                                    onehot[0:TP, c2, c, :], start=False, stop=(chunk == NCH - 1))
                        last.then_inc(sum_ready if c2 else onehot_used, 1)

            def products(u, par, a):
                q = 2 * par + a
                pe.wait_ge(sum_taken, NHOT if isinstance(u, int) and u == 0 else sums_before(u))
                pe.wait_ge(turned_taken, 2 * NB * u + (a + 1) * NB)
                for b in range(GB):
                    reached(pe, quads_taken_v, 2 * GB * u + a * GB + b - 1)
                    reached(pe, quads_taken_s, 2 * GB * u + a * GB + b - 1)
                    for g in range(GQ):
                        four = feats[:, q, 4 * (b * GQ + g):4 * (b * GQ + g + 1), :]
                        last = nc.tensor.matmul(quads[:, b % 2, g, 0:4 * (NF - 1)], four.rearrange("p s f -> p (s f)"),
                                                four[:, :, 1:NF], start=True, stop=True)
                    last.then_inc(quads_ready, 1)

            def layers(u, par, j, n, bank):
                def group(g, terms):
                    pe.wait_ge(sum_taken, n + g - 1)
                    for k, (lhs, rhs) in enumerate(terms):
                        last = nc.tensor.matmul(sums[0:lhs.shape[1], (bank + g) % 2, 0:UNIT], lhs, rhs,
                                                start=(k == 0), stop=(k == len(terms) - 1))
                    last.then_inc(sum_ready, 1)

                dense_t = feats[:, 2 * par:2 * par + 2, :, 0]
                pe.wait_ge(z_loaded[par], 16 * len(RUNS) * (j + 1))
                for o in range(O1):
                    cols = slice(o * P, (o + 1) * P)
                    group(o, [(w1[:, 0, cols], dense_t)]
                          + [(w1[0:ZP, 1 + c, cols], z[0:ZP, par, c, :]) for c in range(ZCH)])
                pe.wait_ge(sum_taken, n + O1)
                for o in range(O2):
                    group(O1 + o, [(w2[:, c, o * P:(o + 1) * P], h1[:, c, :]) for c in range(O1)])
                pe.wait_ge(sum_taken, n + O1 + O2)
                group(O1 + O2, [(w3[:, c:c + 1], h2[:, c, :]) for c in range(O2)])

            pe.wait_ge(rownum_ready, 1)
            pe.wait_ge(ident_ready, 1)
            pe.wait_ge(hot_ready, NHOT)
            lookups(0, 0, 0)
            transposes(0, 0, 0)
            lookups(1, NHOT, NHOT)
            pe.wait_ge(pad_ready, 2)
            products(0, 0, 0)
            transposes(0, 0, 1)
            products(0, 0, 1)
            pe.wait_ge(w_loaded, 16 * 7)
            pe.wait_ge(w1_merged, 1)

            def step(u, par, j, more):
                n, bank = sums_before(u), sums_before(par) % 2
                transposes(u, par, 0)
                if more:
                    lookups(u + 1, n, bank)
                    n, bank = n + NHOT, bank + NHOT
                products(u, par, 0)
                transposes(u, par, 1)
                layers(u - 1, 1 - par, j - 1 + par, n, bank)
                products(u, par, 1)

            with pe.Fori(0, (NU - 2) // 2) as i:
                step(2 * i + 1, 1, i, True)
                step(2 * i + 2, 0, i + 1, True)
            step(NU - 1, 1, NU // 2 - 1, False)
            n = sums_before(NU - 1) + GROUPS
            layers(NU - 1, 1, NU // 2 - 1, n, n)

        def take_quads(eng, copy, taken, samples, u, a):
            for b in range(GB):
                eng.wait_ge(quads_ready, 2 * GB * u + a * GB + b + 1)
                if b == 0:
                    reached(eng, gram_stored, 64 * u + 32 * a)
                for s in samples:
                    block_s = quads[32 * s:32 * s + NF - 1, b % 2, :, s * (NF - 1):(s + 1) * (NF - 1)]
                    at = 4 * b * GQ + s
                    last = copy(gram[0:NF - 1, :, at:at + 4 * GQ - s:4], block_s.rearrange("p g m -> p m g"))
                last.then_inc(taken, 1)

        @block.vector
        def _(dve):
            nc.vector.memset(y[0:1, :], 0.0).then_inc(y_free, 16)
            nc.vector.memset(feats[:, 0:2, :, NF:SLOT], 0.0).then_inc(pad_ready, 1)
            for t in range(NHOT):
                dve.wait_ge(hi_ready, t + 1)
                nc.vector.tensor_tensor(hot_lo[0:TP, t, :, :].rearrange("p c d -> p (c d)"), stage(t),
                                        hot_hi[0:TP, t, :, :].rearrange("p c d -> p (c d)").bitcast(F32),
                                        ALU.subtract).then_inc(hot_ready, 1)

            dve.wait_ge(hot_ready, NHOT)
            nc.vector.memset(feats[:, 2:4, :, NF:SLOT], 0.0).then_inc(pad_ready, 1)

            def make_onehots(u, n):
                dve.wait_ge(hot_ids_loaded, 16 * u + 16)
                for t in range(NHOT):
                    for c2 in range(2):
                        if c2 == 0:
                            reached(dve, onehot_used, NHOT * u + t)
                        else:
                            reached(dve, sum_ready, n + t)
                        for c in range(HC):
                            chunk = c2 * HC + c
                            last = nc.vector.tensor_scalar(onehot[0:TP, c2, c, :], hot_ids[0:TP, t, :],
                                                           row_number[0:TP, chunk:chunk + 1], None, ALU.is_equal)
                        last.then_inc(onehot_ready, 1)

            def step(u, more):
                if more:
                    make_onehots(u + 1, NHOT if isinstance(u, int) and u == 0 else sums_before(u))
                for a in range(2):
                    take_quads(dve, nc.vector.tensor_copy, quads_taken_v, (0, 1), u, a)

            dve.wait_ge(rownum_ready, 1)
            make_onehots(0, 0)
            step(0, True)
            dve.wait_ge(w_loaded, 16 * 7)
            nc.vector.tensor_tensor(w1[:, 0, :], w1[:, 0, :], w1_tail[:, :], ALU.add).then_inc(w1_merged, 1)
            with dve.Fori(0, (NU - 2) // 2) as i:
                step(2 * i + 1, True)
                step(2 * i + 2, True)
            step(NU - 1, False)

        @block.scalar
        def _(act):
            def take_turned(u, par, a):
                for k, batch in enumerate(BATCHES):
                    act.wait_ge(turned_ready, 2 * NB * u + a * NB + k + 1)
                    nc.scalar.activation(features(2 * par + a, batch[0], len(batch)),
                                         turned[:, (a * NB + k) % 2, 0:len(batch), :], ACT.Copy
                                         ).then_inc(turned_taken, 1)

            def take_lookups(u, par, n, bank):
                for t in range(NHOT):
                    act.wait_ge(sum_ready, n + t + 1)
                    nc.scalar.activation(feats[:, 2 * par:2 * par + 2, :, 1 + NCOLD + t],
                                         sums[:, (bank + t) % 2, 0:UNIT].rearrange("p (a s) -> p a s", a=2), ACT.Copy
                                         ).then_inc(sum_taken, 1)

            def take_layers(u, n, bank):
                def group(g, out_ap, m, func, **more):
                    act.wait_ge(sum_ready, n + g + 1)
                    nc.scalar.activation(out_ap, sums[0:m, (bank + g) % 2, 0:UNIT], func, **more
                                         ).then_inc(sum_taken, 1)
                for o in range(O1):
                    group(o, h1[:, o, :], P, ACT.Relu, bias=bias1[:, o:o + 1])
                for o in range(O2):
                    group(O1 + o, h2[:, o, :], P, ACT.Relu, bias=bias2[:, o:o + 1])
                act.wait_ge(y_free, 16 * u + 16)
                group(O1 + O2, y[0:1, :], 1, ACT.Copy)
                act.wait_ge(sum_taken, n + GROUPS)
                act.dma_start(out[bass.ds(u * UNIT, UNIT), :].rearrange("n o -> o n"), y[0:1, :]
                              ).then_inc(y_free, 16)

            def take_products(u, a):
                take_quads(act, lambda o, i: nc.scalar.activation(o, i, ACT.Copy), quads_taken_s, (2, 3), u, a)

            for t in range(NHOT):
                act.wait_ge(staged[t], 16)
                nc.scalar.activation(hot_hi[0:TP, t, :, :].rearrange("p c d -> p (c d)"), stage(t), ACT.Copy
                                     ).then_inc(hi_ready, 1)
            take_lookups(0, 0, 0, 0)
            take_turned(0, 0, 0)
            act.wait_ge(hot_ready, NHOT)
            take_lookups(1, 1, NHOT, NHOT)
            take_products(0, 0)
            take_turned(0, 0, 1)
            take_products(0, 1)
            act.wait_ge(w_loaded, 16 * 7)

            def step(u, par, more):
                n, bank = sums_before(u), sums_before(par) % 2
                take_turned(u, par, 0)
                if more:
                    take_lookups(u + 1, 1 - par, n, bank)
                    n, bank = n + NHOT, bank + NHOT
                take_products(u, 0)
                take_turned(u, par, 1)
                take_layers(u - 1, n, bank)
                take_products(u, 1)

            with act.Fori(0, (NU - 2) // 2) as i:
                step(2 * i + 1, 1, True)
                step(2 * i + 2, 0, True)
            step(NU - 1, 1, False)
            n = sums_before(NU - 1) + GROUPS
            take_layers(NU - 1, n, n)
            act.wait_ge(y_free, 16 * NU + 16)


def kernel(**inputs):
    import numpy as np
    import concourse.bacc as bacc
    from concourse.bass_utils import run_bass_kernel_spmd as run

    nc = bacc.Bacc("TRN2", target_bir_lowering=False, num_devices=1)
    arrays = {}

    def given(name, a):
        a = np.ascontiguousarray(a)
        arrays[name] = a
        return nc.dram_tensor(name, a.shape, mybir.dt.from_np(a.dtype), kind="ExternalInput").ap()

    B = inputs["r_dense_features"].shape[0]
    dense = given("dense", inputs["r_dense_features"])
    ids = given("ids", inputs["ids"])
    ids_by_table = given("ids_by_table", np.asarray(inputs["ids"]).T[list(HOT)])
    tables = [given(f"table{t}", inputs[f"tbl_{t}"]) for t in range(NTAB)]
    W1 = np.asarray(inputs["W_top1"])
    order = list(range(P)) + pair_rows() + list(range(P + NPAIR, 2 * P + NPAIR))
    W1 = given("W1", W1[order])
    W2 = given("W2", inputs["W_top2"])
    b1, b2, W3 = (given(n, np.asarray(inputs[n]).reshape(-1, P).T) for n in ("b_top1", "b_top2", "W_top3"))
    out = nc.dram_tensor("out", [B, 1], F32, kind="ExternalOutput").ap()
    dlrm(nc, dense, ids, ids_by_table, tables, W1, b1, W2, b2, W3, out)
    return run(nc, [arrays], core_ids=[0]).results[0]["out"]
```

```python
from contextlib import ExitStack

import concourse.bass as bass
from concourse import mybir

F32 = mybir.dt.float32
F32R = mybir.dt.float32r
I32 = mybir.dt.int32
U32 = mybir.dt.uint32
ALU = mybir.AluOpType
ACT = mybir.ActivationFunctionType

P = 128
SUB = 128
UNIT = 2 * SUB
HOT = (0, 5, 9, 10, 11, 13, 17)
NTAB = 26
NF = NTAB + 1
COLD = tuple(t for t in range(NTAB) if t not in HOT)
ORDER = tuple(1 + t for t in COLD) + (0,) + tuple(1 + t for t in HOT)
NCOLD, NHOT = len(COLD), len(HOT)
NPAIR = NF * (NF - 1) // 2
ZCH = 3
ZP = NPAIR // ZCH
PB = 4
BATCHES = [list(range(k, min(k + PB, NCOLD + 1))) for k in range(0, NCOLD + 1, PB)]
NB = len(BATCHES)
DENSE = NCOLD
COLD_IN = [len([f for f in b if f != DENSE]) for b in BATCHES]
SLOT = 32
MROWS = 3 * SLOT + NF - 1
QUADS = SUB // 4
GQ = 8
GB = QUADS // GQ
STEP = ("G0 G1 T0 G2 G3 T1 L0 L1 G4 G5 T2 G6 G7 L2 T3 D0 L3 H0 T4 H1 L4 T5 H2 L5 T6 H3 L6 T7 H4 H5 "
        "T8 H6 T9").split()
VECTOR_STEP = "G0 G1 G2 L0 G3 L1 G4 G5 L2 G6 G7 L3 L4 L5 L6".split()
LOW = NF // 2


def pair_rows():
    at, k = {}, P
    for a in range(NF):
        for b in range(a + 1, NF):
            at[a, b] = k
            k += 1
    return [at[min(ORDER[n], ORDER[m]), max(ORDER[n], ORDER[m])] for n in range(NF) for m in range(n + 1, NF)]


def pair_runs():
    runs, at = [], 0
    for n in range(NF - 1):
        m, left = n, NF - 1 - n
        while left:
            k = min(left, ZP - at % ZP)
            runs.append((n, m, at // ZP, at % ZP, k))
            at, m, left = at + k, m + k, left - k
    return runs


RUNS = pair_runs()
EARLY = 14
LATE = 19


def reached(eng, semaphore, value):
    if not isinstance(value, int) or value > 0:
        eng.wait_ge(semaphore, value)


def items(kinds, step=STEP):
    return [(x[0], int(x[1:])) for x in step if x[0] in kinds]


def sum_items(kinds):
    n, out = 0, []
    for kind, k in items(kinds):
        out.append((kind, k, n))
        n += kind in "LDH"
    return out


def settle(eng, passed):
    eng.sem_inc(passed, 1)


def dlrm(nc, dense, ids, ids_by_table, tables, W1, b1, W2, b2, W3, out):
    B, D = dense.shape
    H1, H2 = W2.shape
    O1, O2 = H1 // P, H2 // P
    NU = B // UNIT
    GROUPS = 1 + O1 + O2 + 1
    assert items("T") == [("T", k) for k in range(2 * NB)] and items("G") == [("G", k) for k in range(2 * GB)]
    assert items("L") == [("L", k) for k in range(NHOT)] and items("DH") == [("D", 0)] + [("H", k) for k in range(GROUPS - 1)]
    CH = {t: -(-tables[t].shape[0] // P) for t in HOT}
    assert len(set(CH.values())) == 1
    NCH = CH[HOT[0]]
    TP = tables[HOT[0]].shape[0] // NCH
    assert TP * NCH == tables[HOT[0]].shape[0] and D == P
    HC = NCH // 2
    PIECES = 2 * NHOT

    scratch = nc.dram_tensor("gram_scratch", [2, NF - 1, NF - 1, UNIT], F32, kind="Internal").ap()

    with ExitStack() as ctx:
        def sb(name, shape, dt=F32):
            return ctx.enter_context(nc.sbuf_tensor(name, shape, dt))

        def ps(name, shape, dt=F32):
            return ctx.enter_context(nc.psum_tensor(name, shape, dt))

        def sem(name):
            return ctx.enter_context(nc.semaphore(name))

        ident = sb("ident", [P, P])
        row_number = sb("row_number", [P, NCH])
        w1 = sb("w1", [P, 1 + ZCH, H1])
        w2 = sb("w2", [P, O1, H2])
        w3 = sb("w3", [P, O2])
        bias1 = sb("bias1", [P, O1])
        bias2 = sb("bias2", [P, O2])
        hot_hi = sb("hot_hi", [P, NHOT, NCH, D], F32R)
        hot_lo = sb("hot_lo", [P, NHOT, NCH, D], F32R)
        all_ids = sb("all_ids", [P, 2 * NU, NTAB], I32)
        ids_now = sb("ids_now", [P, 2, NTAB], I32)
        rows = sb("rows", [P, 2, 1 + NCOLD, D])
        hot_ids = sb("hot_ids", [P, NHOT, UNIT], I32)
        onehot = sb("onehot", [P, 2, 2, HC, UNIT], F32R)
        feats = sb("feats", [P, 4, SUB, SLOT])
        gram = sb("gram", [P, NF - 1, SUB])
        z = sb("z", [P, 2, ZCH, UNIT])
        dense_rows = sb("dense_rows", [P, 2, D])
        dense_t = sb("dense_t", [P, UNIT])
        h1 = sb("h1", [P, O1, UNIT])
        h2 = sb("h2", [P, O2, UNIT])
        y = sb("y", [1, UNIT])
        w1_tail = h1[:, :, :].rearrange("p c n -> p (c n)")[:, 0:H1]

        turned = ps("turned", [P, 2, PB, P])
        sums = ps("sums", [P, 2, 2 * UNIT])
        quads = ps("quads", [P, 2, GQ, P])

        ident_zero, ident_ready, rownum_ready = sem("ident_zero"), sem("ident_ready"), sem("rownum_ready")
        pad_ready = sem("pad_ready")
        w_loaded = sem("w_loaded")
        w1_merged = sem("w1_merged")
        staged = [sem(f"staged{t}") for t in range(NHOT)]
        hi_ready, hot_ready = sem("hi_ready"), sem("hot_ready")
        sp_passed, pool_passed = sem("sp_passed"), sem("pool_passed")
        ids_loaded, ids_ready = sem("ids_loaded"), sem("ids_ready")
        mlp_dense_loaded = sem("mlp_dense_loaded")
        dense_loaded = [sem(f"dense_loaded{a}") for a in range(2)]
        rows_loaded = [[sem(f"rows_loaded{a}_{k}") for k in range(NB)] for a in range(2)]
        hot_ids_loaded = sem("hot_ids_loaded")
        turned_ready, turned_taken = sem("turned_ready"), sem("turned_taken")
        onehot_ready, onehot_used = sem("onehot_ready"), sem("onehot_used")
        sum_ready, sum_taken = sem("sum_ready"), sem("sum_taken")
        quads_ready, quads_taken_v, quads_taken_s = sem("quads_ready"), sem("quads_taken_v"), sem("quads_taken_s")
        gram_stored = sem("gram_stored")
        z_loaded = [sem("z_loaded0"), sem("z_loaded1")]
        z_rest_loaded = sem("z_rest_loaded")
        y_free = sem("y_free")

        def stage(t):
            per_buffer = SUB * SLOT // (NCH * D)
            at = t % per_buffer * NCH * D
            return feats[0:TP, 2 + t // per_buffer, :, :].rearrange("p s f -> p (s f)")[:, at:at + NCH * D]

        def sums_before(u):
            if isinstance(u, int) and u == 0:
                return NHOT
            return 2 * NHOT + (NHOT + GROUPS) * (u - 1)

        def features(q, first, count):
            return feats[:, q, :, first:first + count].rearrange("p s f -> p f s")

        block = ctx.enter_context(nc.Block())

        @block.sync
        def _(sp):
            def load_hot_ids(u):
                reached(sp, onehot_ready, PIECES * u)
                settle(sp, sp_passed)
                sp.dma_start(hot_ids[0:TP, :, :],
                             ids_by_table[0:NHOT, bass.ds(u * UNIT, UNIT)].unsqueeze(0).to_broadcast([TP, NHOT, UNIT])
                             ).then_inc(hot_ids_loaded, 16)

            def load_dense(u, a):
                reached(sp, turned_ready, 2 * NB * u - 2 * NB + (a + 1) * NB)
                settle(sp, sp_passed)
                sp.dma_start(rows[:, a, DENSE, :], dense[bass.ds(u * UNIT + a * SUB, SUB), :]
                             ).then_inc(dense_loaded[a], 16)

            def load_mlp_dense(u, sums_made):
                sp.wait_ge(sum_ready, sums_made)
                settle(sp, sp_passed)
                sp.dma_start(dense_rows[:, :, :], dense[bass.ds(u * UNIT, UNIT), :].rearrange("(a p) d -> p a d", p=P)
                             ).then_inc(mlp_dense_loaded, 16)

            def load_pairs(par, runs):
                for n, m, c, p, k in runs:
                    sp.dma_start(z[p:p + k, par, c, :], scratch[par, n, m:m + k, :]).then_inc(z_loaded[par], 16)

            def step(u, par, first=False, last=False):
                if not last:
                    load_hot_ids(u + 1)
                if not first:
                    load_pairs(1 - par, RUNS[EARLY:])
                    load_mlp_dense(u - 1, sums_before(u))
                    sp.wait_ge(sum_ready, sums_before(u))
                for a in range(2):
                    sp.wait_ge(quads_taken_v, 2 * GB * u + (a + 1) * GB)
                    sp.wait_ge(quads_taken_s, 2 * GB * u + (a + 1) * GB)
                    settle(sp, sp_passed)
                    for n0, n1 in ((0, LOW), (LOW, NF - 1)):
                        sp.dma_start(scratch[par, n0:n1, n0:, a * SUB:(a + 1) * SUB], gram[n0:n1, n0:, :]
                                     ).then_inc(gram_stored, 16)
                    if not last:
                        load_dense(u + 1, a)
                if last:
                    load_mlp_dense(u, sums_before(u) + 1)
                sp.wait_ge(gram_stored, 64 * u + 64)
                settle(sp, sp_passed)
                load_pairs(par, RUNS[:EARLY])

            sp.dma_start(all_ids[:, :, :], ids.rearrange("(t p) f -> p t f", p=P)).then_inc(ids_loaded, 16)
            load_hot_ids(0)
            load_dense(0, 0)
            load_dense(0, 1)
            for t in range(NHOT):
                sp.dma_start(stage(t), tables[HOT[t]].rearrange("(p c) d -> p (c d)", c=NCH)).then_inc(staged[t], 16)
            sp.dma_start(w1[:, 0, :], W1[0:P, :]).then_inc(w_loaded, 16)
            sp.dma_start(w1_tail[:, :], W1[P + NPAIR:2 * P + NPAIR, :]).then_inc(w_loaded, 16)
            sp.dma_start(w1[0:ZP, 1:1 + ZCH, :], W1[P:P + NPAIR, :].rearrange("(c p) n -> p c n", p=ZP)
                         ).then_inc(w_loaded, 16)
            sp.dma_start(w2[:, :, :], W2.rearrange("(c p) n -> p c n", p=P)).then_inc(w_loaded, 16)
            sp.dma_start(w3[:, :], W3).then_inc(w_loaded, 16)
            sp.dma_start(bias1[:, :], b1).then_inc(w_loaded, 16)
            sp.dma_start(bias2[:, :], b2).then_inc(w_loaded, 16)
            step(0, 0, first=True)
            with sp.Fori(0, (NU - 2) // 2) as i:
                step(2 * i + 1, 1)
                step(2 * i + 2, 0)
            step(NU - 1, 1, last=True)
            load_pairs(1, RUNS[EARLY:LATE])

        @block.gpsimd
        def _(pool):
            nc.gpsimd.memset(ident[:, :], 0.0).then_inc(ident_zero, 1)
            pool.wait_ge(ident_zero, 1)
            nc.gpsimd.affine_select(out=ident[:, :], in_=ident[:, :], compare_op=ALU.not_equal, fill=1.0, base=0,
                                    pattern=[[-1, P]], channel_multiplier=1).then_inc(ident_ready, 1)
            nc.gpsimd.iota(row_number[:, :], pattern=[[1, NCH]], base=0, channel_multiplier=NCH,
                           allow_small_or_imprecise_dtypes=True).then_inc(rownum_ready, 1)

            def step(u):
                for a in range(2):
                    for k in range(NB):
                        reached(pool, rows_loaded[a][k], 16 * COLD_IN[k] * u)
                    nc.gpsimd.tensor_copy(ids_now[:, a, :], all_ids[:, bass.ds(2 * u + a, 1), :].squeeze(1)
                                          ).then_inc(ids_ready, 1)
                    pool.wait_ge(ids_ready, 2 * u + a + 1)
                    settle(pool, pool_passed)
                    for k, batch in enumerate(BATCHES):
                        reached(pool, turned_ready, 2 * NB * u - 2 * NB + a * NB + k + 1)
                        settle(pool, pool_passed)
                        for f in batch:
                            if f == DENSE:
                                continue
                            t = COLD[f]
                            nc.gpsimd.indirect_dma_start(
                                out=rows[:, a, f, :], out_offset=None, in_=tables[t],
                                in_offset=bass.IndirectOffsetOnAxis(ap=ids_now[:, a, t:t + 1].bitcast(U32), axis=0),
                            ).then_inc(rows_loaded[a][k], 16)

            pool.wait_ge(ids_loaded, 16)
            step(0)
            with pool.Fori(1, NU) as u:
                step(u)
            pool.wait_ge(gram_stored, 64 * NU)
            for n, m, c, p, k in RUNS[LATE:]:
                pool.dma_start(z[p:p + k, 1, c, :], scratch[1, n, m:m + k, :]).then_inc(z_rest_loaded, 16)

        @block.tensor
        def _(pe):
            def transposes(u, k):
                a, b = k // NB, k % NB
                if DENSE in BATCHES[b]:
                    pe.wait_ge(dense_loaded[a], 16 * u + 16)
                pe.wait_ge(rows_loaded[a][b], 16 * COLD_IN[b] * (u + 1))
                reached(pe, turned_taken, 2 * NB * u + k - 1)
                for n, f in enumerate(BATCHES[b]):
                    last = nc.tensor.transpose(turned[:, k % 2, n, :], rows[:, a, f, :], ident[:, :])
                last.then_inc(turned_ready, 1)

            def lookup(u, par, t, n, bank):
                reached(pe, sum_taken, n - 1)
                for c2 in range(2):
                    pe.wait_ge(onehot_ready, PIECES * u + 2 * t + c2 + 1)
                    for c in range(HC):
                        chunk = c2 * HC + c
                        pick = onehot[0:TP, (NHOT * par + t) % 2, c2, c, :]
                        nc.tensor.matmul(sums[:, bank, 0:UNIT], hot_hi[0:TP, t, chunk, :], pick,
                                         start=(chunk == 0), stop=False)
                        last = nc.tensor.matmul(sums[:, bank, 0:UNIT], hot_lo[0:TP, t, chunk, :], pick,
                                                start=False, stop=(chunk == NCH - 1))
                    last.then_inc(sum_ready if c2 else onehot_used, 1)

            def products(u, par, b):
                q = 2 * par + b // GB
                if b == 0:
                    pe.wait_ge(sum_taken, sums_before(u))
                    pe.wait_ge(turned_taken, 2 * NB * (u + 1))
                reached(pe, quads_taken_v, 2 * GB * u + b - 1)
                reached(pe, quads_taken_s, 2 * GB * u + b - 1)
                for g in range(GQ):
                    s = 4 * (b % GB * GQ + g)
                    four = feats[:, q, s:s + 4, :]
                    rows_of = four.rearrange("p s f -> p (s f)")[:, 0:MROWS]
                    last = nc.tensor.matmul(quads[0:MROWS, b % 2, g, 0:4 * (NF - 1)], rows_of,
                                            four[:, :, 1:NF], start=True, stop=True)
                last.then_inc(quads_ready, 1)

            def dense_transposes(u, n, bank):
                pe.wait_ge(mlp_dense_loaded, 16 * u + 16)
                pe.wait_ge(sum_taken, n - 1)
                for a in range(2):
                    last = nc.tensor.transpose(sums[:, bank, a * SUB:(a + 1) * SUB], dense_rows[:, a, :], ident[:, :])
                last.then_inc(sum_ready, 1)

            def layer_sum(u, par, j, h, n, bank, final=False):
                if h == 0:
                    if final:
                        pe.wait_ge(z_rest_loaded, 16 * len(RUNS[LATE:]))
                        pe.wait_ge(z_loaded[par], 16 * (len(RUNS) * j + LATE))
                    else:
                        pe.wait_ge(z_loaded[par], 16 * len(RUNS) * (j + 1))
                if h < O1:
                    cols = slice(h * P, (h + 1) * P)
                    terms = [(w1[0:ZP, 1 + c, cols], z[0:ZP, par, c, :]) for c in range(ZCH)]
                    terms.append((w1[:, 0, cols], dense_t[:, :]))
                elif h < O1 + O2:
                    terms = [(w2[:, c, (h - O1) * P:(h - O1 + 1) * P], h1[:, c, :]) for c in range(O1)]
                else:
                    terms = [(w3[:, c:c + 1], h2[:, c, :]) for c in range(O2)]
                pe.wait_ge(sum_taken, n if h in (0, O1, O1 + O2) else n - 1)
                for k, (lhs, rhs) in enumerate(terms):
                    last = nc.tensor.matmul(sums[0:lhs.shape[1], bank, 0:UNIT], lhs, rhs,
                                            start=(k == 0), stop=(k == len(terms) - 1))
                last.then_inc(sum_ready, 1)

            def step(u, par, j, kinds="TLGDH"):
                for kind, k, n in sum_items(kinds):
                    bank = (sums_before(u if isinstance(u, int) else 2 + par) + n) % 2
                    if kind == "T":
                        transposes(u + 1, k)
                    elif kind == "L":
                        lookup(u + 1, 1 - par, k, sums_before(u) + n, bank)
                    elif kind == "G":
                        products(u, par, k)
                    elif kind == "D":
                        dense_transposes(u - 1, sums_before(u) + n, bank)
                    else:
                        layer_sum(u - 1, 1 - par, j - 1 + par, k, sums_before(u) + n, bank)

            pe.wait_ge(rownum_ready, 1)
            pe.wait_ge(ident_ready, 1)
            for t in range(NHOT):
                pe.wait_ge(hot_ready, t + 1)
                lookup(0, 0, t, t, t % 2)
            for k in range(2 * NB):
                transposes(0, k)
            pe.wait_ge(pad_ready, 2)
            step(0, 0, 0, "TLG")
            pe.wait_ge(w_loaded, 16 * 7)
            pe.wait_ge(w1_merged, 1)
            with pe.Fori(0, (NU - 2) // 2) as i:
                step(2 * i + 1, 1, i)
                step(2 * i + 2, 0, i + 1)
            step(NU - 1, 1, NU // 2 - 1, "GDH")
            for kind, k, n in sum_items("DH"):
                n += sums_before(NU - 1) + GROUPS
                if kind == "D":
                    dense_transposes(NU - 1, n, n % 2)
                else:
                    layer_sum(NU - 1, 1, NU // 2 - 1, k, n, n % 2, final=True)

        def take_quads(eng, copy, taken, samples, u, b):
            eng.wait_ge(quads_ready, 2 * GB * u + b + 1)
            if b % GB == 0:
                reached(eng, gram_stored, 64 * u + 32 * (b // GB))
            for s in samples:
                block_s = quads[32 * s:32 * s + NF - 1, b % 2, :, s * (NF - 1):(s + 1) * (NF - 1)]
                at = 4 * (b % GB) * GQ + s
                last = copy(gram[0:NF - 1, :, at:at + 4 * GQ - s:4], block_s.rearrange("p g m -> p m g"))
            last.then_inc(taken, 1)

        @block.vector
        def _(dve):
            nc.vector.memset(y[0:1, :], 0.0).then_inc(y_free, 16)
            nc.vector.memset(feats[:, 0:2, :, NF:SLOT], 0.0).then_inc(pad_ready, 1)
            def make_onehot(u, par, t):
                if t == 0:
                    dve.wait_ge(hot_ids_loaded, 16 * u + 16)
                for c2 in range(2):
                    reached(dve, onehot_used, NHOT * u + t - 1 + c2)
                    for c in range(HC):
                        chunk = c2 * HC + c
                        last = nc.vector.tensor_scalar(onehot[0:TP, (NHOT * par + t) % 2, c2, c, :],
                                                       hot_ids[0:TP, t, :], row_number[0:TP, chunk:chunk + 1], None,
                                                       ALU.is_equal)
                    last.then_inc(onehot_ready, 1)

            def step(u, par, kinds="LG"):
                for kind, k in items(kinds, VECTOR_STEP):
                    if kind == "L":
                        make_onehot(u + 1, 1 - par, k)
                    else:
                        take_quads(dve, nc.vector.tensor_copy, quads_taken_v, (0, 1), u, k)

            dve.wait_ge(rownum_ready, 1)
            for t in range(NHOT):
                dve.wait_ge(hi_ready, t + 1)
                nc.vector.tensor_tensor(hot_lo[0:TP, t, :, :].rearrange("p c d -> p (c d)"), stage(t),
                                        hot_hi[0:TP, t, :, :].rearrange("p c d -> p (c d)").bitcast(F32),
                                        ALU.subtract).then_inc(hot_ready, 1)
                make_onehot(0, 0, t)
            dve.wait_ge(hot_ready, NHOT)
            nc.vector.memset(feats[:, 2:4, :, NF:SLOT], 0.0).then_inc(pad_ready, 1)
            dve.wait_ge(w_loaded, 16 * 7)
            nc.vector.tensor_tensor(w1[:, 0, :], w1[:, 0, :], w1_tail, ALU.add).then_inc(w1_merged, 1)
            step(0, 0)
            with dve.Fori(0, (NU - 2) // 2) as i:
                step(2 * i + 1, 1)
                step(2 * i + 2, 0)
            step(NU - 1, 1, "G")

        @block.scalar
        def _(act):
            def take_turned(u, par, k):
                a, batch = k // NB, BATCHES[k % NB]
                act.wait_ge(turned_ready, 2 * NB * u + k + 1)
                nc.scalar.activation(features(2 * par + a, batch[0], len(batch)), turned[:, k % 2, 0:len(batch), :],
                                     ACT.Copy).then_inc(turned_taken, 1)

            def take_lookup(par, t, n, bank):
                act.wait_ge(sum_ready, n + 1)
                nc.scalar.activation(feats[:, 2 * par:2 * par + 2, :, 1 + NCOLD + t],
                                     sums[:, bank, 0:UNIT].rearrange("p (a s) -> p a s", a=2), ACT.Copy
                                     ).then_inc(sum_taken, 1)

            def take_dense(n, bank):
                act.wait_ge(sum_ready, n + 1)
                nc.scalar.activation(dense_t[:, :], sums[:, bank, 0:UNIT], ACT.Copy).then_inc(sum_taken, 1)

            def take_layer(u, h, n, bank):
                act.wait_ge(sum_ready, n + 1)
                if h < O1:
                    o, bias = h1[:, h, :], bias1[:, h:h + 1]
                elif h < O1 + O2:
                    o, bias = h2[:, h - O1, :], bias2[:, h - O1:h - O1 + 1]
                else:
                    act.wait_ge(y_free, 16 * u + 16)
                    nc.scalar.activation(y[0:1, :], sums[0:1, bank, 0:UNIT], ACT.Copy).then_inc(sum_taken, 1)
                    act.wait_ge(sum_taken, n + 1)
                    act.dma_start(out[bass.ds(u * UNIT, UNIT), :].rearrange("n o -> o n"), y[0:1, :]
                                  ).then_inc(y_free, 16)
                    return
                nc.scalar.activation(o, sums[:, bank, 0:UNIT], ACT.Relu, bias=bias).then_inc(sum_taken, 1)

            def step(u, par, kinds="TLGDH"):
                for kind, k, n in sum_items(kinds):
                    bank = (sums_before(u if isinstance(u, int) else 2 + par) + n) % 2
                    if kind == "T":
                        take_turned(u + 1, 1 - par, k)
                    elif kind == "L":
                        take_lookup(1 - par, k, sums_before(u) + n, bank)
                    elif kind == "G":
                        take_quads(act, lambda o, i: nc.scalar.activation(o, i, ACT.Copy), quads_taken_s, (2, 3), u, k)
                    elif kind == "D":
                        take_dense(sums_before(u) + n, bank)
                    else:
                        take_layer(u - 1, k, sums_before(u) + n, bank)

            for t in range(NHOT):
                act.wait_ge(staged[t], 16)
                nc.scalar.activation(hot_hi[0:TP, t, :, :].rearrange("p c d -> p (c d)"), stage(t), ACT.Copy
                                     ).then_inc(hi_ready, 1)
            for t in range(NHOT):
                take_lookup(0, t, t, t % 2)
            for k in range(2 * NB):
                take_turned(0, 0, k)
            act.wait_ge(hot_ready, NHOT)
            step(0, 0, "TLG")
            act.wait_ge(w_loaded, 16 * 7)
            act.wait_ge(w1_merged, 1)
            with act.Fori(0, (NU - 2) // 2) as i:
                step(2 * i + 1, 1)
                step(2 * i + 2, 0)
            step(NU - 1, 1, "GDH")
            for kind, k, n in sum_items("DH"):
                n += sums_before(NU - 1) + GROUPS
                if kind == "D":
                    take_dense(n, n % 2)
                else:
                    take_layer(NU - 1, k, n, n % 2)
            act.wait_ge(y_free, 16 * NU + 16)


def kernel(**inputs):
    import numpy as np
    import concourse.bacc as bacc
    from concourse.bass_utils import run_bass_kernel_spmd as run

    nc = bacc.Bacc("TRN2", target_bir_lowering=False, num_devices=1)
    arrays = {}

    def given(name, a):
        a = np.ascontiguousarray(a)
        arrays[name] = a
        return nc.dram_tensor(name, a.shape, mybir.dt.from_np(a.dtype), kind="ExternalInput").ap()

    B = inputs["r_dense_features"].shape[0]
    dense = given("dense", inputs["r_dense_features"])
    ids = given("ids", inputs["ids"])
    ids_by_table = given("ids_by_table", np.asarray(inputs["ids"]).T[list(HOT)])
    tables = [given(f"table{t}", inputs[f"tbl_{t}"]) for t in range(NTAB)]
    W1 = np.asarray(inputs["W_top1"])
    order = list(range(P)) + pair_rows() + list(range(P + NPAIR, 2 * P + NPAIR))
    W1 = given("W1", W1[order])
    W2 = given("W2", inputs["W_top2"])
    b1, b2, W3 = (given(n, np.asarray(inputs[n]).reshape(-1, P).T) for n in ("b_top1", "b_top2", "W_top3"))
    out = nc.dram_tensor("out", [B, 1], F32, kind="ExternalOutput").ap()
    dlrm(nc, dense, ids, ids_by_table, tables, W1, b1, W2, b2, W3, out)
    return run(nc, [arrays], core_ids=[0]).results[0]["out"]
```

```python
from contextlib import ExitStack

import concourse.bass as bass
from concourse import mybir

F32 = mybir.dt.float32
F32R = mybir.dt.float32r
I32 = mybir.dt.int32
U32 = mybir.dt.uint32
ALU = mybir.AluOpType
ACT = mybir.ActivationFunctionType

P = 128
SUB = 128
UNIT = 2 * SUB
HOT = (0, 5, 9, 10, 11, 13, 17)
NTAB = 26
NF = NTAB + 1
COLD = tuple(t for t in range(NTAB) if t not in HOT)
ORDER = tuple(1 + t for t in COLD) + (0,) + tuple(1 + t for t in HOT)
NCOLD, NHOT = len(COLD), len(HOT)
NPAIR = NF * (NF - 1) // 2
ZCH = 3
ZP = NPAIR // ZCH
CIRCLE = (NF - 1) // 2
ZN = NF // ZCH
WIDE = NF + CIRCLE
PB = 4
BATCHES = [list(range(k, min(k + PB, NCOLD))) for k in range(0, NCOLD, PB)]
NB = len(BATCHES)
DENSE = NCOLD
SLOT = 32
MROWS = 3 * SLOT + NF
QUADS = SUB // 4
GQ = 8
GB = QUADS // GQ
AHEAD = 2
STEP = ("G4 G5 G6 T0 G7 L2 T1 L3 L4 T2 L5 L6 T3 H0 H1 D0 T4 I0 H2 H3 T5 "
        "G0 G1 T6 H4 G2 T7 H5 G3 T8 A0 T9 I1 A1 H6").split()
VECTOR_STEP = "L2 G4 G5 L3 G6 G7 L4 L5 L6 A0 G0 A1 G1 G2 W0 G3".split()
FIRST = ("S0 S1 S2 L0 S3 L1 S4 L2 S5 L3 T0 S6 T1 L4 T2 L5 T3 D0 T4 I0 L6 T5 P0 "
         "G0 G1 T6 G2 G3 T7 A0 T8 A1 T9 I1").split()
STORES = ((0, CIRCLE + 1, 1, NF, 1),
          (CIRCLE + 1, NF, CIRCLE + 2, NF, CIRCLE + 2),
          (CIRCLE + 1, NF, NF, WIDE, 0))


def pair_rows():
    at, k = {}, P
    for a in range(NF):
        for b in range(a + 1, NF):
            at[a, b] = k
            k += 1
    pairs = [(ORDER[n], ORDER[(n + d) % NF]) for n in range(NF) for d in range(1, CIRCLE + 1)]
    return [at[min(p), max(p)] for p in pairs]


def reached(eng, semaphore, value):
    if not isinstance(value, int) or value > 0:
        eng.wait_ge(semaphore, value)


def items(kinds, step=STEP):
    return [(x[0], int(x[1:])) for x in step if x[0] in kinds]


def sum_items(kinds, step=STEP):
    n, out = 0, []
    for kind, k in items(kinds, step):
        out.append((kind, k, n))
        n += kind in "LHA"
    return out


def settle(eng, passed):
    eng.sem_inc(passed, 1)


def dlrm(nc, dense_by_dim, ids, ids_by_table, tables, W1, b1, W2, b2, W3, out):
    D, B = dense_by_dim.shape
    H1, H2 = W2.shape
    O1, O2 = H1 // P, H2 // P
    NU = B // UNIT
    NSUM = O1 + O2 + 1
    assert O2 == 2 and O1 <= 4
    assert ZN <= STORES[0][1]
    for kind, start, count in (("T", 0, 2 * NB), ("A", 0, AHEAD), ("L", AHEAD, NHOT - AHEAD), ("H", 0, NSUM)):
        assert items(kind) == [(kind, start + k) for k in range(count)]
    assert STEP.index("A0") > STEP.index(f"H{NSUM - 2}")
    assert items("G") == [("G", (GB + k) % (2 * GB)) for k in range(2 * GB)]
    CH = {t: -(-tables[t].shape[0] // P) for t in HOT}
    assert len(set(CH.values())) == 1
    NCH = CH[HOT[0]]
    TP = tables[HOT[0]].shape[0] // NCH
    assert TP * NCH == tables[HOT[0]].shape[0] and D == P
    HC = NCH // 2
    PIECES = 2 * NHOT

    scratch = nc.dram_tensor("gram_scratch", [2, NF * (WIDE + 1) + 1, SUB], F32, kind="Internal").ap()
    blocks = [scratch[a, 0:NF * WIDE, :].rearrange("(n w) s -> n w s", w=WIDE) for a in range(2)]

    with ExitStack() as ctx:
        def sb(name, shape, dt=F32):
            return ctx.enter_context(nc.sbuf_tensor(name, shape, dt))

        def ps(name, shape, dt=F32):
            return ctx.enter_context(nc.psum_tensor(name, shape, dt))

        def sem(name):
            return ctx.enter_context(nc.semaphore(name))

        ident = sb("ident", [P, P])
        row_number = sb("row_number", [P, NCH])
        w1 = sb("w1", [P, 1 + ZCH, H1])
        w2 = sb("w2", [P, O1, H2])
        w3 = sb("w3", [P, O2])
        ones = sb("ones", [P, 1])
        bias1 = sb("bias1", [P, O1])
        bias2 = sb("bias2", [P, O2])
        hot_hi = sb("hot_hi", [P, NHOT, NCH, D], F32R)
        hot_lo = sb("hot_lo", [P, NHOT, NCH, D], F32R)
        all_ids = sb("all_ids", [P, 2 * NU, NTAB], I32)
        ids_now = sb("ids_now", [P, 2, NTAB], I32)
        rows = sb("rows", [P, 2, NCOLD, D])
        hot_ids = sb("hot_ids", [P, NHOT, UNIT], I32)
        onehot = sb("onehot", [P, 2, 2, HC, UNIT], F32R)
        feats = sb("feats", [P, 4, SUB, SLOT])
        gram = sb("gram", [P, NF, SUB])
        z = sb("z", [P, ZCH, UNIT])
        dense_t = sb("dense_t", [P, 2, UNIT])
        h1 = sb("h1", [P, O1, UNIT])
        h2 = sb("h2", [P, O2, UNIT])
        weighed = sb("weighed", [P, UNIT])
        y = sb("y", [P, 2 * NU])
        w1_tail = h1[:, :, :].rearrange("p c n -> p (c n)")[:, 0:H1]

        turned = ps("turned", [P, 2, PB, P])
        sums = ps("sums", [P, 2, 2 * UNIT])
        quads = ps("quads", [P, 2, GQ, P])
        last_sums = [quads[:, h // 2, h % 2 * GQ // 2, :] for h in range(O1)]

        ident_zero, ident_ready, rownum_ready = sem("ident_zero"), sem("ident_ready"), sem("rownum_ready")
        pad_ready, ones_ready = sem("pad_ready"), sem("ones_ready")
        w_loaded = sem("w_loaded")
        w1_merged = sem("w1_merged")
        staged = [sem(f"staged{t}") for t in range(NHOT)]
        hi_ready, hot_ready = sem("hi_ready"), sem("hot_ready")
        sp_passed, pool_passed = sem("sp_passed"), sem("pool_passed")
        ids_loaded, ids_ready = sem("ids_loaded"), sem("ids_ready")
        dense_loaded = sem("dense_loaded")
        rows_loaded = [[sem(f"rows_loaded{a}_{k}") for k in range(NB)] for a in range(2)]
        hot_ids_loaded = sem("hot_ids_loaded")
        turned_ready, turned_taken = sem("turned_ready"), sem("turned_taken")
        onehot_ready, onehot_used = sem("onehot_ready"), sem("onehot_used")
        sum_ready, sum_taken = sem("sum_ready"), sem("sum_taken")
        weighed_part, weighed_ready = sem("weighed_part"), sem("weighed_ready")
        quads_ready, quads_taken_v, quads_taken_s = sem("quads_ready"), sem("quads_taken_v"), sem("quads_taken_s")
        gram_stored = sem("gram_stored")
        last_rows_stored = sem("last_rows_stored")
        z_loaded = [sem("z_loaded0"), sem("z_loaded1")]
        last_z_loaded = [sem(f"last_z_loaded{c}") for c in range(ZCH)]
        out_stored = sem("out_stored")

        def stage(t):
            per_buffer = SUB * SLOT // (NCH * D)
            at = t % per_buffer * NCH * D
            return feats[0:TP, 2 + t // per_buffer, :, :].rearrange("p s f -> p (s f)")[:, at:at + NCH * D]

        def sums_before(u):
            fewer = AHEAD if isinstance(u, int) and u == NU - 1 else 0
            return NHOT + AHEAD + (NHOT + NSUM) * u - fewer

        def sum_done(u, kind, k):
            return sums_before(u) + next(n for a, b, n in sum_items("LHA") if (a, b) == (kind, k)) + 1

        def features(q, first, count):
            return feats[:, q, :, first:first + count].rearrange("p s f -> p f s")

        block = ctx.enter_context(nc.Block())

        @block.sync
        def _(sp):
            def load_hot_ids(u):
                reached(sp, onehot_ready, PIECES * u)
                settle(sp, sp_passed)
                sp.dma_start(hot_ids[0:TP, :, :],
                             ids_by_table[0:NHOT, bass.ds(u * UNIT, UNIT)].unsqueeze(0).to_broadcast([TP, NHOT, UNIT])
                             ).then_inc(hot_ids_loaded, 16)

            def load_dense(u, par):
                sp.dma_start(dense_t[:, par, :], dense_by_dim[:, bass.ds(u * UNIT, UNIT)]).then_inc(dense_loaded, 16)

            def load_pairs(a, c, loaded):
                at = c * ZN * (WIDE + 1) + 1
                pairs = scratch[a, at:at + ZN * (WIDE + 1), :].rearrange("(n w) s -> n w s", n=ZN)
                sp.dma_start(z[0:ZP, c, a * SUB:(a + 1) * SUB], pairs[:, 0:CIRCLE, :]).then_inc(loaded, 16)

            def store_and_load(u, a, last=False):
                sp.wait_ge(quads_taken_v, 2 * GB * u + (a + 1) * GB)
                sp.wait_ge(quads_taken_s, 2 * GB * u + (a + 1) * GB)
                settle(sp, sp_passed)
                for k, (n0, n1, w0, w1_, m0) in enumerate(STORES):
                    sp.dma_start(blocks[a][n0:n1, w0:w1_, :], gram[n0:n1, m0:m0 + w1_ - w0, :]
                                 ).then_inc(last_rows_stored if last and k == 0 else gram_stored, 16)
                if last:
                    sp.wait_ge(last_rows_stored, 16)
                    load_pairs(a, 0, last_z_loaded[0])
                    sp.wait_ge(gram_stored, 16 * (len(STORES) * (2 * u + a + 1) - 1))
                else:
                    sp.wait_ge(gram_stored, 16 * len(STORES) * (2 * u + a + 1))
                    settle(sp, sp_passed)
                for c in range(1 if last else 0, ZCH):
                    load_pairs(a, c, last_z_loaded[c] if last else z_loaded[a])

            def step(u, par, last=False):
                store_and_load(u, 1)
                load_dense(u + 1, 1 - par)
                if not last:
                    load_hot_ids(u + 2)
                sp.wait_ge(sum_ready, sum_done(u, "H", O1 - 1))
                store_and_load(u + 1, 0)

            sp.dma_start(all_ids[:, :, :], ids.rearrange("(t p) f -> p t f", p=P)).then_inc(ids_loaded, 16)
            load_hot_ids(0)
            load_dense(0, 0)
            for t in range(NHOT):
                sp.dma_start(stage(t), tables[HOT[t]].rearrange("(p c) d -> p (c d)", c=NCH)).then_inc(staged[t], 16)
            sp.dma_start(w1[:, 0, :], W1[0:P, :]).then_inc(w_loaded, 16)
            sp.dma_start(w1_tail[:, :], W1[P + NPAIR:2 * P + NPAIR, :]).then_inc(w_loaded, 16)
            sp.dma_start(w1[0:ZP, 1:1 + ZCH, :], W1[P:P + NPAIR, :].rearrange("(c p) n -> p c n", p=ZP)
                         ).then_inc(w_loaded, 16)
            sp.dma_start(w2[:, :, :], W2.rearrange("(c p) n -> p c n", p=P)).then_inc(w_loaded, 16)
            sp.dma_start(w3[:, :], W3).then_inc(w_loaded, 16)
            sp.dma_start(bias1[:, :], b1).then_inc(w_loaded, 16)
            sp.dma_start(bias2[:, :], b2).then_inc(w_loaded, 16)
            load_hot_ids(1)
            store_and_load(0, 0)
            step(0, 0)
            with sp.Fori(0, NU // 2 - 2) as i:
                step(2 * i + 1, 1)
                step(2 * i + 2, 0)
            step(NU - 3, 1)
            step(NU - 2, 0, last=True)
            store_and_load(NU - 1, 1, last=True)
            sp.wait_ge(sum_taken, sums_before(NU - 1) + 2 * NSUM)
            sp.dma_start(out, y[:, :]).then_inc(out_stored, 16)
            sp.wait_ge(out_stored, 16)

        @block.gpsimd
        def _(pool):
            nc.gpsimd.memset(ident[:, :], 0.0).then_inc(ident_zero, 1)
            pool.wait_ge(ident_zero, 1)
            nc.gpsimd.affine_select(out=ident[:, :], in_=ident[:, :], compare_op=ALU.not_equal, fill=1.0, base=0,
                                    pattern=[[-1, P]], channel_multiplier=1).then_inc(ident_ready, 1)
            nc.gpsimd.iota(row_number[:, :], pattern=[[1, NCH]], base=0, channel_multiplier=NCH,
                           allow_small_or_imprecise_dtypes=True).then_inc(rownum_ready, 1)

            def gather(a, subtile_ids):
                for k, batch in enumerate(BATCHES):
                    for f in batch:
                        t = COLD[f]
                        nc.gpsimd.indirect_dma_start(
                            out=rows[:, a, f, :], out_offset=None, in_=tables[t],
                            in_offset=bass.IndirectOffsetOnAxis(ap=subtile_ids[:, t:t + 1].bitcast(U32), axis=0),
                        ).then_inc(rows_loaded[a][k], 16)

            pool.wait_ge(ids_loaded, 16)
            for a in range(2):
                gather(a, all_ids[:, a, :])
            with pool.Fori(1, NU) as u:
                for a in range(2):
                    pool.wait_ge(ids_ready, 2 * u + a - 1)
                    settle(pool, pool_passed)
                    gather(a, ids_now[:, a, :])

        @block.tensor
        def _(pe):
            def transposes(u, k):
                a, b = k // NB, k % NB
                pe.wait_ge(rows_loaded[a][b], 16 * len(BATCHES[b]) * (u + 1))
                reached(pe, turned_taken, 2 * NB * u + k - 1)
                for n, f in enumerate(BATCHES[b]):
                    last = nc.tensor.transpose(turned[:, k % 2, n, :], rows[:, a, f, :], ident[:, :])
                last.then_inc(turned_ready, 1)

            def lookup(u, par, t, n, bank):
                reached(pe, sum_taken, n - 1)
                for c2 in range(2):
                    pe.wait_ge(onehot_ready, PIECES * u + 2 * t + c2 + 1)
                    for c in range(HC):
                        chunk = c2 * HC + c
                        pick = onehot[0:TP, (NHOT * par + t) % 2, c2, c, :]
                        nc.tensor.matmul(sums[:, bank, 0:UNIT], hot_hi[0:TP, t, chunk, :], pick,
                                         start=(chunk == 0), stop=False)
                        last = nc.tensor.matmul(sums[:, bank, 0:UNIT], hot_lo[0:TP, t, chunk, :], pick,
                                                start=False, stop=(chunk == NCH - 1))
                    last.then_inc(sum_ready if c2 else onehot_used, 1)

            def products(u, par, b):
                q = 2 * par + b // GB
                if b == 0:
                    pe.wait_ge(sum_taken, NHOT if isinstance(u, int) and u == 0 else sum_done(u - 1, "L", NHOT - 1))
                if b % GB == 0:
                    pe.wait_ge(turned_taken, 2 * NB * u + (b // GB + 1) * NB)
                reached(pe, quads_taken_v, 2 * GB * u + b - 1)
                reached(pe, quads_taken_s, 2 * GB * u + b - 1)
                for g in range(GQ):
                    s = 4 * (b % GB * GQ + g)
                    four = feats[:, q, s:s + 4, :]
                    rows_of = four.rearrange("p s f -> p (s f)")[:, 0:MROWS]
                    last = nc.tensor.matmul(quads[0:MROWS, b % 2, g, 0:4 * NF], rows_of,
                                            four[:, :, 0:NF], start=True, stop=True)
                last.then_inc(quads_ready, 1)

            def layer_sum(u, par, h, before, n, bank, subtiles=(0, 1)):
                cols = slice(subtiles[0] * SUB, (subtiles[-1] + 1) * SUB)
                width = len(subtiles) * SUB
                pe.wait_ge(sum_taken, n - 1)
                if h < O1:
                    units = slice(h * P, (h + 1) * P)
                    terms = [(w1[:, 0, units], dense_t[:, par, cols])]
                    terms += [(w1[0:ZP, 1 + c, units], z[0:ZP, c, cols]) for c in range(ZCH)]
                elif h < O1 + O2:
                    terms = [(w2[:, c, (h - O1) * P:(h - O1 + 1) * P], h1[:, c, cols]) for c in range(O1)]
                else:
                    pe.wait_ge(weighed_ready, u + subtiles[0] + 1)
                    for a in subtiles:
                        last = nc.tensor.matmul(sums[:, bank, a:a + 1], weighed[:, a * SUB:(a + 1) * SUB], ones[:, :],
                                                start=True, stop=True)
                    last.then_inc(sum_ready, 1)
                    return
                for k, (lhs, rhs) in enumerate(terms):
                    if h == 0 and k == 1:
                        for a in subtiles:
                            pe.wait_ge(z_loaded[a], 16 * ZCH * (u + 1))
                    if h == O1 and k == O1 - 1:
                        pe.wait_ge(sum_taken, before)
                    last = nc.tensor.matmul(sums[:, bank, 0:width], lhs, rhs,
                                            start=(k == 0), stop=(k == len(terms) - 1))
                last.then_inc(sum_ready, 1)

            def step(u, par, last=False):
                for kind, k, n in sum_items("TLGH" if last else "TLGHA"):
                    bank = (sums_before(par) + n) % 2
                    if kind == "T":
                        transposes(u + 1, k)
                    elif kind == "L":
                        lookup(u + 1, 1 - par, k, sums_before(u) + n, bank)
                    elif kind == "A":
                        lookup(u + 2, par, k, sums_before(u) + n, bank)
                    elif kind == "G":
                        products(u if k >= GB else u + 1, par if k >= GB else 1 - par, k)
                    else:
                        layer_sum(u, par, k, sum_done(u, "H", k - 1) if k else 0, sums_before(u) + n, bank)

            pe.wait_ge(rownum_ready, 1)
            pe.wait_ge(ident_ready, 1)
            for kind, k, n in sum_items("TLGA", FIRST):
                if kind == "T":
                    transposes(0, k)
                elif kind == "L":
                    pe.wait_ge(hot_ready, k + 1)
                    lookup(0, 0, k, n, n % 2)
                elif kind == "A":
                    lookup(1, 1, k, n, n % 2)
                else:
                    if k == 0:
                        pe.wait_ge(pad_ready, 1)
                    products(0, 0, k)
            pe.wait_ge(pad_ready, 2)
            pe.wait_ge(w_loaded, 16 * 7)
            pe.wait_ge(w1_merged, 1)
            step(0, 0)
            with pe.Fori(0, NU // 2 - 2) as i:
                step(2 * i + 1, 1)
                step(2 * i + 2, 0)
            step(NU - 3, 1)
            step(NU - 2, 0, last=True)
            for k in range(GB, 2 * GB):
                products(NU - 1, 1, k)
            def last_first_layer(c):
                pe.wait_ge(last_z_loaded[c], 16)
                for k in range(O1):
                    last = nc.tensor.matmul(last_sums[k], w1[0:ZP, 1 + c, k * P:(k + 1) * P], z[0:ZP, c, SUB:UNIT],
                                            start=False, stop=(c == ZCH - 1))
                    if c == ZCH - 1:
                        last.then_inc(sum_ready, 1)

            for h in range(NSUM):
                n = sums_before(NU - 1) + h
                if h == NSUM - 1:
                    pe.wait_ge(quads_taken_v, 2 * GB * NU)
                    pe.wait_ge(quads_taken_s, 2 * GB * NU)
                    for k in range(O1):
                        nc.tensor.matmul(last_sums[k], w1[:, 0, k * P:(k + 1) * P], dense_t[:, 1, SUB:UNIT],
                                         start=True, stop=False)
                    last_first_layer(0)
                layer_sum(NU - 1, 1, h, n, n, n % 2, (0,))
            for c in range(1, ZCH):
                last_first_layer(c)
            for h in range(O1, NSUM - 1):
                n = sums_before(NU - 1) + NSUM + h
                layer_sum(NU - 1, 1, h, n, n, n % 2, (1,))
            n = sums_before(NU - 1) + 2 * NSUM - 1
            for c in range(O2):
                pe.wait_ge(sum_taken, n - 1 + c)
                last = nc.tensor.matmul(sums[:, n % 2, 1:2], h2[:, c, SUB:UNIT], w3[:, c:c + 1],
                                        start=(c == 0), stop=(c == O2 - 1))
            last.then_inc(sum_ready, 1)

        def take_quads(eng, copy, taken, samples, u, b):
            eng.wait_ge(quads_ready, 2 * GB * u + b + 1)
            if b % GB == 0:
                reached(eng, gram_stored, 16 * len(STORES) * (2 * u + b // GB))
            for s in samples:
                block_s = quads[32 * s:32 * s + NF, b % 2, :, s * NF:(s + 1) * NF]
                at = 4 * (b % GB) * GQ + s
                last = copy(gram[0:NF, :, at:at + 4 * GQ - s:4], block_s.rearrange("p g m -> p m g"))
            last.then_inc(taken, 1)

        @block.vector
        def _(dve):
            nc.vector.memset(ones[:, :], 1.0).then_inc(ones_ready, 1)
            nc.vector.memset(feats[:, 0:2, :, NF:SLOT], 0.0).then_inc(pad_ready, 1)

            def make_onehot(u, par, t):
                if t == 0:
                    dve.wait_ge(hot_ids_loaded, 16 * u + 16)
                for c2 in range(2):
                    if c2 == 0:
                        reached(dve, onehot_used, NHOT * u + t - 1)
                    elif t >= 2:
                        reached(dve, sum_ready, lookup_done(u, t - 2))
                    elif not isinstance(u, int) or u > 0:
                        reached(dve, sum_ready, lookup_done(u - 1, NHOT - 2 + t))
                    for c in range(HC):
                        chunk = c2 * HC + c
                        last = nc.vector.tensor_scalar(onehot[0:TP, (NHOT * par + t) % 2, c2, c, :],
                                                       hot_ids[0:TP, t, :], row_number[0:TP, chunk:chunk + 1], None,
                                                       ALU.is_equal)
                    last.then_inc(onehot_ready, 1)

            def lookup_done(u, t):
                if isinstance(u, int) and u == 0:
                    return t + 1
                if t >= AHEAD:
                    return sum_done(u - 1, "L", t)
                return NHOT + t + 1 if isinstance(u, int) and u == 1 else sum_done(u - 2, "A", t)

            def weigh(weighings, sums_made, subtiles=(0, 1)):
                cols = slice(subtiles[0] * SUB, (subtiles[-1] + 1) * SUB)
                dve.wait_ge(sum_taken, sums_made)
                nc.vector.tensor_scalar(weighed[:, cols], h2[:, 0, cols], w3[:, 0:1], None, ALU.mult
                                        ).then_inc(weighed_part, 1)
                dve.wait_ge(weighed_part, weighings + 1)
                nc.vector.scalar_tensor_tensor(weighed[:, cols], h2[:, 1, cols], w3[:, 1:2], weighed[:, cols],
                                               ALU.mult, ALU.add).then_inc(weighed_ready, 1)

            def take(u, k):
                take_quads(dve, nc.vector.tensor_copy, quads_taken_v, (0, 1), u, k)

            def step(u, par, last=False):
                for kind, k in items("LGW" if last else "LGWA", VECTOR_STEP):
                    if kind == "L":
                        make_onehot(u + 1, 1 - par, k)
                    elif kind == "A":
                        make_onehot(u + 2, par, k)
                    elif kind == "W":
                        weigh(u, sum_done(u, "H", O1 + O2 - 1))
                    else:
                        take(u if k >= GB else u + 1, k)

            dve.wait_ge(rownum_ready, 1)
            for t in range(NHOT):
                dve.wait_ge(hi_ready, t + 1)
                nc.vector.tensor_tensor(hot_lo[0:TP, t, :, :].rearrange("p c d -> p (c d)"), stage(t),
                                        hot_hi[0:TP, t, :, :].rearrange("p c d -> p (c d)").bitcast(F32),
                                        ALU.subtract).then_inc(hot_ready, 1)
                make_onehot(0, 0, t)
            take(0, 0)
            make_onehot(1, 1, 0)
            take(0, 1)
            take(0, 2)
            make_onehot(1, 1, 1)
            take(0, 3)
            dve.wait_ge(w_loaded, 16 * 7)
            nc.vector.tensor_tensor(w1[:, 0, :], w1[:, 0, :], w1_tail, ALU.add).then_inc(w1_merged, 1)
            step(0, 0)
            with dve.Fori(0, NU // 2 - 2) as i:
                step(2 * i + 1, 1)
                step(2 * i + 2, 0)
            step(NU - 3, 1)
            step(NU - 2, 0, last=True)
            for k in range(GB, 2 * GB):
                take(NU - 1, k)
            weigh(NU - 1, sums_before(NU - 1) + O1 + O2, (0,))

        @block.scalar
        def _(act):
            def take_turned(u, par, k):
                a, batch = k // NB, BATCHES[k % NB]
                act.wait_ge(turned_ready, 2 * NB * u + k + 1)
                nc.scalar.activation(features(2 * par + a, batch[0], len(batch)), turned[:, k % 2, 0:len(batch), :],
                                     ACT.Copy).then_inc(turned_taken, 1)

            def place_ids(u, a):
                nc.scalar.activation(ids_now[:, a, :], all_ids[:, bass.ds(2 * u + a, 1), :].squeeze(1), ACT.Copy
                                     ).then_inc(ids_ready, 1)

            def place_dense(u, par):
                act.wait_ge(dense_loaded, 16 * u + 16)
                nc.scalar.activation(feats[:, 2 * par:2 * par + 2, :, DENSE],
                                     dense_t[:, par, :].rearrange("p (a s) -> p a s", a=2), ACT.Copy)

            def take_lookup(par, t, n, bank):
                act.wait_ge(sum_ready, n + 1)
                nc.scalar.activation(feats[:, 2 * par:2 * par + 2, :, 1 + NCOLD + t],
                                     sums[:, bank, 0:UNIT].rearrange("p (a s) -> p a s", a=2), ACT.Copy
                                     ).then_inc(sum_taken, 1)

            def take_layer(u, h, n, bank, subtiles=(0, 1), last=False):
                cols = slice(subtiles[0] * SUB, (subtiles[-1] + 1) * SUB)
                width = len(subtiles) * SUB
                act.wait_ge(sum_ready, n + 1)
                if h < O1:
                    o, bias = h1[:, h, cols], bias1[:, h:h + 1]
                elif h < O1 + O2:
                    o, bias = h2[:, h - O1, cols], bias2[:, h - O1:h - O1 + 1]
                else:
                    nc.scalar.activation(y[:, bass.ds(2 * u + subtiles[0], len(subtiles))],
                                         sums[:, bank, subtiles[0]:subtiles[-1] + 1], ACT.Copy).then_inc(sum_taken, 1)
                    return
                made = last_sums[h] if last and h < O1 else sums[:, bank, 0:width]
                nc.scalar.activation(o, made, ACT.Relu, bias=bias).then_inc(sum_taken, 1)

            def take(u, k):
                take_quads(act, lambda o, i: nc.scalar.activation(o, i, ACT.Copy), quads_taken_s, (2, 3), u, k)

            def step(u, par, last=False):
                for kind, k, n in sum_items("TLGHD" if last else "TLGHDIA"):
                    bank = (sums_before(par) + n) % 2
                    if kind == "T":
                        take_turned(u + 1, 1 - par, k)
                    elif kind == "D":
                        place_dense(u + 1, 1 - par)
                    elif kind == "I":
                        place_ids(u + 2, k)
                    elif kind == "L":
                        take_lookup(1 - par, k, sums_before(u) + n, bank)
                    elif kind == "A":
                        take_lookup(par, k, sums_before(u) + n, bank)
                    elif kind == "G":
                        take(u if k >= GB else u + 1, k)
                    else:
                        take_layer(u, k, sums_before(u) + n, bank)

            act.wait_ge(ones_ready, 1)
            nc.scalar.activation(y[:, 0:1], ones[:, :], ACT.Copy)
            act.wait_ge(ids_loaded, 16)
            for kind, k, n in sum_items("STLGDAIP", FIRST):
                if kind == "S":
                    act.wait_ge(staged[k], 16)
                    nc.scalar.activation(hot_hi[0:TP, k, :, :].rearrange("p c d -> p (c d)"), stage(k), ACT.Copy
                                         ).then_inc(hi_ready, 1)
                elif kind == "T":
                    take_turned(0, 0, k)
                elif kind == "D":
                    place_dense(0, 0)
                elif kind == "I":
                    place_ids(1, k)
                elif kind == "L":
                    take_lookup(0, k, n, n % 2)
                elif kind == "A":
                    take_lookup(1, k, n, n % 2)
                elif kind == "P":
                    act.wait_ge(hot_ready, NHOT)
                    act.wait_ge(pad_ready, 1)
                    nc.scalar.activation(feats[:, 2:4, :, NF:SLOT], feats[:, 0:2, :, NF:SLOT], ACT.Copy
                                         ).then_inc(pad_ready, 1)
                else:
                    take(0, k)
            act.wait_ge(w_loaded, 16 * 7)
            act.wait_ge(w1_merged, 1)
            step(0, 0)
            with act.Fori(0, NU // 2 - 2) as i:
                step(2 * i + 1, 1)
                step(2 * i + 2, 0)
            step(NU - 3, 1)
            step(NU - 2, 0, last=True)
            for k in range(GB, 2 * GB):
                take(NU - 1, k)
            for a in range(2):
                for h in range(NSUM):
                    n = sums_before(NU - 1) + a * NSUM + h
                    take_layer(NU - 1, h, n, n % 2, (a,), last=(a == 1))

def kernel(**inputs):
    import numpy as np
    import concourse.bacc as bacc
    from concourse.bass_utils import run_bass_kernel_spmd as run

    nc = bacc.Bacc("TRN2", target_bir_lowering=False, num_devices=1)
    arrays = {}

    def given(name, a):
        a = np.ascontiguousarray(a)
        arrays[name] = a
        return nc.dram_tensor(name, a.shape, mybir.dt.from_np(a.dtype), kind="ExternalInput").ap()

    B = inputs["r_dense_features"].shape[0]
    dense_by_dim = given("dense_by_dim", np.asarray(inputs["r_dense_features"]).T)
    ids = given("ids", inputs["ids"])
    ids_by_table = given("ids_by_table", np.asarray(inputs["ids"]).T[list(HOT)])
    tables = [given(f"table{t}", inputs[f"tbl_{t}"]) for t in range(NTAB)]
    W1 = np.asarray(inputs["W_top1"])
    order = list(range(P)) + pair_rows() + list(range(P + NPAIR, 2 * P + NPAIR))
    W1 = given("W1", W1[order])
    W2 = given("W2", inputs["W_top2"])
    b1, b2, W3 = (given(n, np.asarray(inputs[n]).reshape(-1, P).T) for n in ("b_top1", "b_top2", "W_top3"))
    out = nc.dram_tensor("out", [P, B // P], F32, kind="ExternalOutput").ap()
    dlrm(nc, dense_by_dim, ids, ids_by_table, tables, W1, b1, W2, b2, W3, out)
    return run(nc, [arrays], core_ids=[0]).results[0]["out"].T.reshape(B, 1)
```
